# Optimizing a Trainium2 kernel written in Bass

```python
import numpy as np
import jax
import jax.numpy as jnp

def _softmax(x, axis=-1):
    return jax.nn.softmax(x, axis=axis)

def _gelu(x):
    return jax.nn.gelu(x, approximate=True)

def _silu(x):
    return jax.nn.silu(x)

def _sigmoid(x):
    return jax.nn.sigmoid(x)

def _layernorm(x, axis=-1, eps=1e-05):
    m = jnp.mean(x, axis=axis, keepdims=True)
    v = jnp.var(x, axis=axis, keepdims=True)
    return (x - m) / jnp.sqrt(v + eps)

def _scatter_add(tgt, idx, src, axis=0):
    return tgt.at[idx].add(src)

def _segment_sum(src, seg, n):
    return jax.ops.segment_sum(src, seg, n)
kernel_name = 'mk_adaln_d1_jaxref_r2_8eb56f'

def setup_inputs(seed: int=0):
    np.random.seed(seed)
    _w = jnp.asarray

    def _L0_attn_setup():
        import jax, jax.numpy as jnp
        import numpy as np
        DIM = 512
        EPS = 1e-12

        def _rmsnorm(x, gamma):
            norm = jnp.sqrt(jnp.sum(x * x, axis=-1, keepdims=True))
            scale = jnp.asarray(np.sqrt(x.shape[-1]), x.dtype)
            return x / jnp.maximum(norm, EPS) * scale * gamma
        key = jax.random.key(seed)
        k1, k2, k3 = jax.random.split(key, 3)
        b, n, d = (2, 2048, DIM)
        x = jax.random.normal(k1, (b, n, d), dtype=jnp.float32)
        w_qkva = jax.random.normal(k2, (3 * d, d), dtype=jnp.float32) * (1.0 / np.sqrt(d))
        gamma = jnp.ones((d,), dtype=jnp.float32)
        return {'x': x, 'gamma': gamma, 'w_qkva': w_qkva}
    _L0_attn_in = _L0_attn_setup()

    def _L0_ffn_setup():
        import jax, jax.numpy as jnp
        import numpy as np
        K = 2
        CAP_FACTOR = 1.25
        key = jax.random.key(seed)
        ks = jax.random.split(key, 6)
        B, T, C, H, E = (8, 1024, 512, 2048, 8)
        return {'x': jax.random.normal(ks[0], (B, T, C), dtype=jnp.float32), 'Wr': jax.random.normal(ks[1], (C, E), dtype=jnp.float32) * 0.02, 'W1': jax.random.normal(ks[2], (E, C, H), dtype=jnp.float32) * 0.02, 'b1': jax.random.normal(ks[3], (E, H), dtype=jnp.float32) * 0.02, 'W2': jax.random.normal(ks[4], (E, H, C), dtype=jnp.float32) * 0.02, 'b2': jax.random.normal(ks[5], (E, C), dtype=jnp.float32) * 0.02}
    _L0_ffn_in = _L0_ffn_setup()
    _L0_c = _w((lambda *s: np.random.randn(*s).astype(np.float32) * 0.05)(4, 512))
    _L0_wmod = _w((lambda *s: np.random.randn(*s).astype(np.float32) * 0.05)(512, 6 * 512) * 512 ** (-0.5))
    _d = {'L0_attn_x': _L0_attn_in['x'], 'L0_attn_gamma': _L0_attn_in['gamma'], 'L0_attn_w_qkva': _L0_attn_in['w_qkva'], 'L0_ffn_Wr': _L0_ffn_in['Wr'], 'L0_ffn_W1': _L0_ffn_in['W1'], 'L0_ffn_b1': _L0_ffn_in['b1'], 'L0_ffn_W2': _L0_ffn_in['W2'], 'L0_ffn_b2': _L0_ffn_in['b2'], 'L0_c': _L0_c, 'L0_wmod': _L0_wmod}
    _x0 = _d['L0_attn_x']
    _d['L0_attn_x'] = jax.random.normal(jax.random.fold_in(jax.random.key(seed), 1), (4, 2048, 512), dtype=_x0.dtype)
    del _x0
    return _d

def reference(L0_attn_x, L0_attn_gamma, L0_attn_w_qkva, L0_ffn_Wr, L0_ffn_W1, L0_ffn_b1, L0_ffn_W2, L0_ffn_b2, L0_c, L0_wmod):

    def _L0_attn_ref(x, gamma, w_qkva):
        import jax, jax.numpy as jnp
        import numpy as np
        DIM = 512
        EPS = 1e-12

        def _rmsnorm(x, gamma):
            norm = jnp.sqrt(jnp.sum(x * x, axis=-1, keepdims=True))
            scale = jnp.asarray(np.sqrt(x.shape[-1]), x.dtype)
            return x / jnp.maximum(norm, EPS) * scale * gamma
        d = x.shape[-1]
        xn = _rmsnorm(x, gamma)
        qkva = jnp.einsum('bnd,ed->bne', xn, w_qkva)
        q, kv, a = (qkva[..., :d], qkva[..., d:2 * d], qkva[..., 2 * d:])
        a = jax.nn.sigmoid(a)

        def binary_operator(e_i, e_j):
            a_i, kv_i = e_i
            a_j, kv_j = e_j
            return (a_j * a_i, a_j * kv_i + kv_j)
        _, kv_scan = jax.lax.associative_scan(binary_operator, (a, kv), axis=1)
        return q * kv_scan

    def _L0_ffn_ref(x, Wr, W1, b1, W2, b2):
        import jax, jax.numpy as jnp
        import numpy as np
        K = 2
        CAP_FACTOR = 1.25
        B, T, C = x.shape
        E = Wr.shape[1]
        capacity = int(T / E * CAP_FACTOR)
        probs = jax.nn.softmax(x @ Wr, axis=-1)
        topk_probs, topk_experts = jax.lax.top_k(probs, K)
        S = T * K
        e_flat = topk_experts.reshape(B, S)
        p_flat = topk_probs.reshape(B, S)
        x_rep = jnp.repeat(x, K, axis=1)
        onehot = jax.nn.one_hot(e_flat, E, dtype=jnp.int32)
        pos_all = jnp.cumsum(onehot, axis=1) - onehot
        pos = jnp.take_along_axis(pos_all, e_flat[..., None], axis=-1)[..., 0]
        keep = pos < capacity
        pos_c = jnp.minimum(pos, capacity - 1)
        b_idx = jnp.broadcast_to(jnp.arange(B)[:, None], (B, S))
        buf = jnp.zeros((E, B, capacity, C), dtype=x.dtype)
        buf = buf.at[e_flat, b_idx, pos_c].add(x_rep * keep[..., None].astype(x.dtype))
        h = jax.nn.relu(jnp.einsum('ebnc,ech->ebnh', buf, W1) + b1[:, None, None, :])
        y = jnp.einsum('ebnh,ehc->ebnc', h, W2) + b2[:, None, None, :]
        y_tok = y[e_flat, b_idx, pos_c]
        y_tok = y_tok * keep[..., None].astype(x.dtype) * p_flat[..., None]
        out = y_tok.reshape(B, T, K, C).sum(axis=2)
        return out
    x = L0_attn_x
    mod = (_silu(L0_c) @ L0_wmod).reshape(L0_c.shape[0], 6, 1, -1)
    sa, ca, ga, sb, cb, gb = (mod[:, 0], mod[:, 1], mod[:, 2], mod[:, 3], mod[:, 4], mod[:, 5])
    ga = (2 * (ga >= 0) - 1) * jnp.maximum(jnp.abs(ga), 0.25)
    gb = (2 * (gb >= 0) - 1) * jnp.maximum(jnp.abs(gb), 0.25)
    h = _layernorm(x, axis=-1) * (1 + ca) + sa
    x = x + ga * _L0_attn_ref(h, L0_attn_gamma, L0_attn_w_qkva)
    h = _layernorm(x, axis=-1) * (1 + cb) + sb
    x = x + gb * _L0_ffn_ref(h, L0_ffn_Wr, L0_ffn_W1, L0_ffn_b1, L0_ffn_W2, L0_ffn_b2)
    return x

_drawn_inputs = setup_inputs


def setup_inputs(seed=0):
    import zlib

    import numpy as np

    out = dict(_drawn_inputs(seed))
    spreads = {'L0_attn_gamma': (1.0, 0.2)}
    factors = {'L0_ffn_Wr': 4.154,
     'L0_ffn_W1': 4.39,
     'L0_ffn_b1': 8.0,
     'L0_ffn_W2': 3.63,
     'L0_ffn_b2': 26.619}
    for name, (base, spread) in spreads.items():
        noise = np.random.default_rng([zlib.crc32(name.encode()), seed]).standard_normal(out[name].shape)
        drawn = base * np.exp(spread * noise) if base else spread * noise
        out[name] = jnp.asarray(drawn.astype(out[name].dtype))
    for name, factor in factors.items():
        out[name] = (out[name] * factor).astype(out[name].dtype)
    return out
```

```python
from contextlib import ExitStack

import concourse.bass as bass
from concourse import mybir

ALU = mybir.AluOpType
ACT = mybir.ActivationFunctionType
AX = mybir.AxisListType.X
F32 = mybir.dt.float32
F16 = mybir.dt.float16
I32 = mybir.dt.int32
ABSMAX = bass.bass_isa.ReduceOp.absmax

P = 128
B, T, D = 4, 2048, 512
TOKENS = B * T
KC = D // P
E = 8
H = 2048
HC = H // P
CAP = int(T / E * 1.25)
SLOTS = B * CAP
NSLOTS = E * SLOTS
BLK = 512
TB = BLK // P
NB = TOKENS // BLK
BPB = T // BLK
UNIT = 2 * CAP
UT = UNIT // P
ROW = 2 * D + 8
META = D
KEXP = 4
HID_SHIFT = 2.0 ** -9
B1_SHIFT = 2.0 ** -18
TINY = 2.0 ** -100
FAR = 1.0e6
MODW = 6 * D + 8
NRT = 34
MOD_LINKS = 20
WLINKS = 20
START_LINKS = 29
EXPONENT = 0x7F800000


def build_program(nc, x, gamma, wq, wr, w1, b1, w2, b2, ct, wmod, out):
    xf = x.rearrange("b t d -> (b t) d")
    rows = nc.dram_tensor("slot_rows", [NSLOTS, ROW // 2], I32, kind="Internal").ap()
    mod_rows = nc.dram_tensor("mod_rows", [B, MODW], F32, kind="Internal").ap()

    with ExitStack() as ctx:
        def sb(name, shape, dt):
            return ctx.enter_context(nc.sbuf_tensor(name, shape, dt))

        def sem(name):
            return ctx.enter_context(nc.semaphore(name))

        def sems(name, n):
            return [sem(f"{name}{i}") for i in range(n)]

        reg_a = sb("reg_a", [P, 2 * KC * H], F16)
        reg_b = sb("reg_b", [P, 2 * HC * D], F16)
        reg_c = sb("reg_c", [P, 2 * HC * UNIT], F16)
        reg_d = sb("reg_d", [P, 4 * 2048], F32)
        reg_e = sb("reg_e", [P, 15392], F32)

        w1s = reg_a[:, :].rearrange("p (s c h) -> p s c h", s=2, c=KC)
        w2s = reg_b[:, :].rearrange("p (s c d) -> p s c d", s=2, c=HC)
        hid = reg_c[:, :].rearrange("p (s c n) -> p s c n", s=2, c=HC)
        stage = reg_d[:, :].rearrange("p (q n) -> p q n", q=4)
        xbuf = reg_b[:, :].bitcast(F32).rearrange("p (s t d) -> p s t d", s=4, t=TB)
        wqs = reg_c[:, 0:8 * 3 * D].rearrange("p (s c e) -> p s c e", s=2, c=KC)
        xns = reg_c[:, 8 * 3 * D:8 * 3 * D + 16 * BLK].rearrange("p (u s c n) -> p u s c n", u=2, s=2, c=KC)
        wmod_hi = reg_a[:, :].bitcast(F32).rearrange("p (q n) -> p q n", q=4)

        at = [0]

        def part(words):
            at[0] += words
            return reg_e[:, at[0] - words:at[0]]

        h1 = part(TB * D).rearrange("p (t d) -> p t d", t=TB)
        h2 = part(TB * D).rearrange("p (t d) -> p t d", t=TB)
        row = part(2 * TB * ROW // 2).bitcast(F16).rearrange("p (u t n) -> p u t n", u=2, t=TB)
        sig = part(2 * BLK).rearrange("p (u n) -> p u n", u=2)
        scn = part(2 * BLK).rearrange("p (u n) -> p u n", u=2)
        yT = part(KC * BLK).rearrange("p (c n) -> p c n", c=KC)
        mods = part(4 * D).rearrange("p (m d) -> p m d", m=4)
        h2T = part(2 * D).bitcast(F16).rearrange("p (u c n) -> p u c n", u=2, c=8)
        rowf = row.rearrange("p u t n -> p (u t n)").bitcast(F32).rearrange("p (u t n) -> p u t n", u=2, t=TB)
        assert at[0] == 15392
        wq_raw = reg_e[:, 2 * TB * D:2 * TB * D + KC * 3 * D].rearrange("p (c e) -> p c e", c=KC)
        modr = reg_a[:, :].bitcast(F32)[:, 2 * 2048:2 * 2048 + MODW]
        modt = reg_e[:, TB * D:TB * D + 2 * D]
        at[0] = 0
        xT = part(8 * UNIT).bitcast(F16).rearrange("p (u c n) -> p u c n", u=2, c=8)
        grow = part(UT * ROW // 2).bitcast(F16).rearrange("p (t n) -> p t n", t=UT)
        growf = grow.rearrange("p t n -> p (t n)").bitcast(F32).rearrange("p (t n) -> p t n", t=UT)
        gbt = part(6 * D).rearrange("p (v k d) -> p v k d", v=2, k=3)
        b2t = part(D)
        yv = part(2 * D).rearrange("p (u d) -> p u d", u=2)
        yo = part(2 * D).rearrange("p (u d) -> p u d", u=2)
        rt = part(4 * CAP).rearrange("p (u n) -> p u n", u=4)
        assert at[0] <= 15392

        rowi = rowf.rearrange("p u t n -> p (u t n)").bitcast(I32).rearrange("p (u t n) -> p u t n", u=2, t=TB)
        growi = growf.rearrange("p t n -> p (t n)").bitcast(I32).rearrange("p (t n) -> p t n", t=UT)
        zrow = sb("zrow", [P, ROW // 2], I32)
        zid = sb("zid", [P, 1], I32)
        ident32 = sb("ident32", [P, P], F32)
        ident16 = sb("ident16", [P, P], F16)
        upper = sb("upper", [P, P], F16)
        ones = sb("ones", [P, P], F16)
        junk = sb("junk", [P, BLK], mybir.dt.bfloat16)
        cts = sb("cts", [P, KC, B], F32)
        csig = sb("csig", [P, KC, B], F32)
        silc = sb("silc", [P, KC, B], F32)
        gam = sb("gam", [P, KC], F32)
        gams = sb("gams", [P, KC], F32)
        wrr = sb("wrr", [P, KC, E], F32)
        wrs = sb("wrs", [P, 2, KC, E], F16)
        gaS = sb("gaS", [P, KC, B], F32)
        cga = sb("cga", [P, KC], F32)
        irT = sb("irT", [P, B], F32)
        ir = sb("ir", [P, 1], F32)
        shb = sb("shb", [P, B, 2], F32)
        shb9 = sb("shb9", [P, B], F32)
        shmax = sb("shmax", [P, 1], F32)
        ishk = sb("ishk", [P, 2, 3], F32)
        inv2 = sb("inv2", [P, 2, 3], F32)
        mx0 = sb("mx0", [P, 4], F32)
        mg0 = sb("mg0", [P, 4], F32)
        ex0 = sb("ex0", [P, 4], F32)
        sc0 = sb("sc0", [P, 4], F32)
        is0 = sb("is0", [P, 4], F32)
        iq = sb("iq", [P, 2], F32)
        mrow = sb("mrow", [P, 4], F32)
        half = sb("half", [P, TB], F32)
        st1 = sb("st1", [P, TB, 6], F32)
        sm1 = sb("sm1", [P, 6, TB], F32)
        st2 = sb("st2", [P, TB, 6], F32)
        sm2 = sb("sm2", [P, 6, TB], F32)
        rs1 = sb("rs1", [P, TB], F32)
        rs2 = sb("rs2", [P, TB], F32)
        ss1 = sb("ss1", [P, TB], F32)
        rp1 = sb("rp1", [P, TB], F32)
        rn1 = sb("rn1", [P, TB], F32)
        carry = sb("carry", [P, KC], F32)
        rev = sb("rev", [P, TB, E], F32)
        base = sb("base", [P, E], F32)
        lgt = sb("lgt", [P, TB, E], F32)
        prb = sb("prb", [P, TB, E], F32)
        prm = sb("prm", [P, TB, E], F32)
        eqt = sb("eqt", [P, TB, E], F32)
        wgt = sb("wgt", [P, TB, E], F32)
        oh1 = sb("oh1", [P, TB, E], F32)
        oh2 = sb("oh2", [P, TB, E], F32)
        mh = sb("mh", [P, TB, E], F16)
        cm = sb("cm", [P, E], F16)
        cs = sb("cs", [P, E], F32)
        rv = sb("rv", [P, 8, TB], F32)
        slf = sb("slf", [P, 2, TB], F32)
        sli = sb("sli", [P, 2, TB], I32)
        idi = sb("idi", [P, TB], I32)
        idf = sb("idf", [P, TB], F32)
        ecur = sb("ecur", [P, 1], F32)
        meta = sb("meta", [P, 2, UT, 3], F32)
        midx = sb("midx", [P, 2, UT], I32)
        gt = sb("gt", [P, 3, UT], F32)
        b1r = sb("b1r", [P, HC], F32)
        b1s = sb("b1s", [P, B, HC], F32)
        wmx = sb("wmx", [P, 8], F32)
        wmg = sb("wmg", [P, 2], F32)
        wex = sb("wex", [P, 2], F32)
        wsc = sb("wsc", [P, 2], F32)
        wis = sb("wis", [P, 2], F32)
        bank = [ctx.enter_context(nc.psum_tensor(f"bank{i}", [P, 512], F32)) for i in range(8)]
        bank_a, bank_kv, bank_q, bank_t, bank_r = bank[0], bank[1:3], bank[3:5], bank[5:7], bank[7]
        bank_t16 = [b[:, :].bitcast(F16).rearrange("p (c n) -> p c n", c=8) for b in bank_t]
        bank_h, bank_y = bank[0:4], [bank[4], bank[7]]

        s_const = sem("s_const")
        s_zrow = sem("s_zrow")
        s_cd = sem("s_cd")
        s_small = sem("s_small")
        s_wmod = sems("s_wmod", 6)
        s_wqraw = sem("s_wqraw")
        s_csig = sem("s_csig")
        s_silc = sem("s_silc")
        s_modmm = sem("s_modmm")
        s_dch = sem("s_dch")
        s_modw = sem("s_modw")
        s_max0 = sem("s_max0")
        s_gat = sem("s_gat")
        s_shb = sem("s_shb")
        s_wqhi = sem("s_wqhi")
        s_wqlo = sem("s_wqlo")
        s_init = sem("s_init")
        s_x = sems("s_xin", 4)
        s_ma = sem("s_ma")
        s_mb = sem("s_mb")
        s_bn1 = sem("s_bn1")
        s_l1 = sem("s_l1")
        s_r1 = sem("s_r1")
        s_z1 = sem("s_z1")
        s_hm1 = sem("s_hm1")
        s_ha1 = sem("s_ha1")
        s_sq = sem("s_sq")
        s_rp = sem("s_rp")
        s_rn = sem("s_rn")
        s_xn = sem("s_xn")
        s_t1 = sem("s_t1")
        s_xhi = sem("s_xhi")
        s_xlo = sem("s_xlo")
        s_qkv = sem("s_qkv")
        s_sig = sem("s_sig")
        s_scn = sem("s_scn")
        s_car = sem("s_car")
        s_y = sem("s_y")
        s_cga = sem("s_cga")
        s_t2 = sem("s_t2")
        s_x2 = sem("s_x2")
        s_out = sems("s_out", 4)
        s_bn2 = sem("s_bn2")
        s_l2 = sem("s_l2")
        s_r2 = sem("s_r2")
        s_z2 = sem("s_z2")
        s_hm2 = sem("s_hm2")
        s_ha2 = sem("s_ha2")
        s_rhi = sem("s_rhi")
        s_rlo = sem("s_rlo")
        s_t3 = sem("s_t3")
        s_ht = sem("s_ht")
        s_lg = sem("s_lg")
        s_ex = sem("s_ex")
        s_rt = sem("s_rt")
        s_pos = sem("s_pos")
        s_send = sems("s_send", 2)
        s_sent = sem("s_sent")
        s_stg = sems("s_stg", 4)
        s_b1 = sem("s_b1")
        s_b2 = sem("s_b2")
        s_gb = sem("s_gb")
        s_wall = sem("s_wall")
        s_wch = sem("s_wch")
        s_whi = sem("s_whi")
        s_wlo = sem("s_wlo")
        s_b1s = sem("s_b1s")
        s_inv = sem("s_inv")
        s_g = sem("s_g")
        s_tg = sem("s_tg")
        s_xt = sem("s_xt")
        s_meta = sem("s_meta")
        s_gate = sem("s_gate")
        s_mm1 = sem("s_mm1")
        s_r = sem("s_r")
        s_hhi = sem("s_hhi")
        s_hlo = sem("s_hlo")
        s_mm2 = sem("s_mm2")
        s_yd = sem("s_yd")
        s_yo = sem("s_yo")
        s_add = sems("s_add", 2)
        s_added = sem("s_added")

        s_passed = sem("s_passed")

        block = ctx.enter_context(nc.Block())

        def wait(eng, s, value):
            if isinstance(value, int) and value <= 0:
                return
            eng.wait_ge(s, value)

        def wait_alone(eng, s, value):
            wait(eng, s, value)
            eng.sem_inc(s_passed, 1)

        def attn_steps(eng, step):
            for i in (0, 1):
                step(0, i, i)
            with eng.Fori(0, 3) as b:
                for k in range(2, 6):
                    step(b + k // 4, k % 4, None)
            for i in range(14, NB + 2):
                step(i // 4, i % 4, i)

        def has(i, off):
            return i is None or 0 <= i + off < NB

        def rel(q, j, off):
            return q + (j + off) // 4, (j + off) % 4

        def tok(ap, n):
            return ap[bass.ds(n * BLK, BLK), :].rearrange("(t p) d -> p t d", p=P)

        def slot_rows(v):
            return rows[bass.ds(v * UNIT, UNIT), :].rearrange("(t p) n -> p t n", p=P)

        @block.sync
        def _(sp):
            def load_x(q, j):
                sp.dma_start(xbuf[:, j, :, :], tok(xf, 4 * q + j)).then_inc(s_x[j], 16)

            def load_mod(q, k, s):
                src = mod_rows[bass.ds(q, 1), k * D:(k + 2) * D].to_broadcast([P, 2 * D])
                dst = mods[:, (0 if k == 0 else 2):(2 if k == 0 else 4), :].rearrange("p m d -> p (m d)")
                sp.dma_start(dst, src).then_inc(s, 16)

            sp.dma_start(cts[:, :, :], ct).then_inc(s_small, 16)
            sp.dma_start(gam[:, :], gamma).then_inc(s_small, 16)
            sp.dma_start(wrr[:, :, :], wr).then_inc(s_small, 16)
            load_x(0, 0)
            wm = wmod.rearrange("(c p) n -> p c n", p=P)
            for m in range(6):
                dst = (stage[:, m, :] if m < 4 else wmod_hi[:, m - 4, :]).rearrange("p (c n) -> p c n", c=KC)
                sp.dma_start(dst, wm[:, :, m * D:(m + 1) * D]).then_inc(s_wmod[m], 16)
                if m == 1:
                    sp.dma_start(wq_raw, wq.rearrange("(c p) e -> p c e", p=P)).then_inc(s_wqraw, 16)
            load_x(0, 1)
            load_x(0, 2)
            load_x(0, 3)
            sp.wait_ge(s_dch, MOD_LINKS)
            sp.dma_start(mod_rows[:, :], modr[0:B, :]).then_inc(s_modw, 16)
            sp.wait_ge(s_modw, 16)
            load_mod(0, 0, s_ma)
            load_mod(0, 3, s_mb)
            sp.dma_start(shb[:, :, :], mod_rows[:, 6 * D:6 * D + 2].unsqueeze(0).to_broadcast([P, B, 2])).then_inc(s_shb, 16)
            sp.wait_ge(s_modmm, 6)
            for c in range(KC):
                sp.dma_start(stage[:, c, :], w1[0, c * P:(c + 1) * P, :]).then_inc(s_stg[c], 16)
            sp.dma_start(b1r[:, :], b1[0, :, :]).then_inc(s_b1, 16)
            sp.wait_ge(s_zrow, 1)
            for e in range(E):
                sp.dma_start(rows[e * SLOTS:(e + 1) * SLOTS, :].rearrange("(t p) n -> p t n", p=P),
                             zrow[:, :].unsqueeze(1).to_broadcast([P, SLOTS // P, ROW // 2])).then_inc(s_init, 16)
            sp.dma_start(out[TOKENS:TOKENS + P, :], zrow[:, :].bitcast(F32)[:, 0:D]).then_inc(s_init, 16)

            def step(q, j, i):
                n = 4 * q + j
                if has(i, -1):
                    pq, pj = rel(q, j, -1)
                    wait(sp, s_x2, TB * n)
                    sp.dma_start(tok(out, n - 1), xbuf[:, pj, :, :]).then_inc(s_out[pj], 16)
                if has(i, -2) and has(i, 2):
                    oq, oj = rel(q, j, -2)
                    wait_alone(sp, s_out[oj], 16 * (oq + 1))
                    wait_alone(sp, s_z2, TB * (n - 1))
                    load_x(oq + 1, oj)
                if j == 2 and (i is None or i + 2 < NB):
                    wait(sp, s_ha1, TB * (n + 2))
                    load_mod(q + 1, 0, s_ma)
                if j == 0 and has(i, 0) and i != 0:
                    wait(sp, s_ha2, TB * n)
                    load_mod(q, 3, s_mb)

            def experts():
                for k in range(4):
                    sp.wait_ge(s_out[k], 16 * BPB)
                for k in range(2):
                    sp.wait_ge(s_send[k], 16 * 2 * TB * NB // 2)
                sp.dma_start(growi, slot_rows(0)).then_inc(s_g, 16)
                for v in range(2):
                    for k, (p0, p1, b) in ((0, (0, P, 0)), (1, (0, P // 2, 0)), (1, (P // 2, P, 1)), (2, (0, P, 1))):
                        sp.dma_start(gbt[p0:p1, v, k, :], mod_rows[2 * v + b:2 * v + b + 1, 5 * D:6 * D]
                                     .to_broadcast([p1 - p0, D])).then_inc(s_gb, 16)
                sp.wait_ge(s_tg, UT)
                sp.wait_ge(s_meta, 1)
                sp.dma_start(growi, slot_rows(1)).then_inc(s_g, 16)
                with sp.Fori(0, E) as e:
                    nxt = (e + 1) % E
                    for c in range(4):
                        wait(sp, s_wlo, 8 * e + c + 1)
                        sp.dma_start(stage[:, c, :].rearrange("p (c d) -> p c d", c=4),
                                     w2[bass.ds(e, 1), c * 4 * P:(c + 1) * 4 * P, :]
                                     .rearrange("a (c p) d -> p (a c) d", p=P)).then_inc(s_stg[c], 16)
                    wait(sp, s_b1s, e + 1)
                    sp.dma_start(b1r[:, :], b1[bass.ds(nxt, 1), :, :].rearrange("a p c -> p (a c)")).then_inc(s_b1, 16)
                    wait(sp, s_yd, 2 * UT * e + 2)
                    sp.dma_start(b2t, b2[bass.ds(e, 1), :].to_broadcast([P, D])).then_inc(s_b2, 16)
                    for c in range(4):
                        wait(sp, s_wlo, 8 * e + 4 + c + 1)
                        sp.dma_start(stage[:, c, :], w1[bass.ds(nxt, 1), c * P:(c + 1) * P, :]
                                     .rearrange("a p h -> p (a h)")).then_inc(s_stg[c], 16)
                    for u in range(2):
                        wait(sp, s_tg, UT * (2 * e + u + 2))
                        wait_alone(sp, s_meta, 2 * e + u + 2)
                        sp.dma_start(growi, slot_rows((2 * e + u + 2) % (2 * E))).then_inc(s_g, 16)
                sp.wait_ge(s_g, 16 * (2 * E + 2))
                sp.wait_ge(s_b1, 16 * (E + 1))
                for c in range(4):
                    sp.wait_ge(s_stg[c], 16 * (2 * E + 1))

            attn_steps(sp, step)
            experts()

        @block.gpsimd
        def _(pool):
            g = nc.gpsimd
            pool.sem_inc(s_added, 2)
            pool.sem_inc(s_sent, 1)
            g.memset(ident32[:, :], 0.0).then_inc(s_const, 1)
            g.memset(ident16[:, :], 0.0).then_inc(s_const, 1)
            g.memset(upper[:, :], 1.0).then_inc(s_const, 1)
            g.iota(idi[:, :], [[P, TB]], base=0, channel_multiplier=1).then_inc(s_const, 1)
            g.memset(zrow[:, :], 0).then_inc(s_const, 1)
            pool.wait_ge(s_const, 5)
            g.iota(zid[:, :], [[1, 1]], base=TOKENS, channel_multiplier=1).then_inc(s_const, 1)
            for m in (ident32, ident16):
                g.affine_select(out=m[:, :], in_=m[:, :], compare_op=ALU.not_equal, fill=1.0, base=0,
                                pattern=[[-1, P]], channel_multiplier=1).then_inc(s_const, 1)
            g.affine_select(out=upper[:, :], in_=upper[:, :], compare_op=ALU.is_ge, fill=0.0, base=-1,
                            pattern=[[1, P]], channel_multiplier=-1).then_inc(s_const, 1)
            g.memset(half[:, :], -0.5).then_inc(s_const, 1)
            pool.wait_ge(s_max0, 3)
            g.partition_all_reduce(mg0[:, 0:3], mx0[:, 0:3], P, ABSMAX).then_inc(s_max0, 1)
            pool.wait_ge(s_const, 10)

            def rstd(n, s_link, s_done, src, dst):
                wait(pool, s_link, 7 * n + 7)
                g.tensor_tensor(dst[:, :], src[:, 5, :], half[:, :], ALU.pow).then_inc(s_done, 1)

            def modulate(n, h, m, s_z, s_m, s_a):
                for t in range(TB):
                    wait(pool, s_z, TB * n + t + 1)
                    g.tensor_tensor(h[:, t, :], h[:, t, :], mods[:, m + 1, :], ALU.mult).then_inc(s_m, 1)
                for t in range(TB):
                    wait(pool, s_m, TB * n + t + 1)
                    g.tensor_tensor(h[:, t, :], h[:, t, :], mods[:, m, :], ALU.add).then_inc(s_a, 1)

            def ln1_h(q, j):
                n = 4 * q + j
                rstd(n, s_l1, s_r1, sm1, rs1)
                if j == 0:
                    wait(pool, s_ma, 16 * (q + 1))
                modulate(n, h1, 0, s_z1, s_hm1, s_ha1)

            def ln1_norm(n):
                wait(pool, s_sq, TB * n + TB)
                g.tensor_tensor(rp1[:, :], ss1[:, :], half[:, :], ALU.pow).then_inc(s_rp, 1)

            def step(q, j, i):
                n = 4 * q + j
                if has(i, 1):
                    ln1_norm(n + 1)
                if has(i, -1):
                    pq, pj = rel(q, j, -1)
                    rstd(n - 1, s_l2, s_r2, sm2, rs2)
                    if pj == 0:
                        wait(pool, s_mb, 16 * (pq + 1))
                    modulate(n - 1, h2, 2, s_z2, s_hm2, s_ha2)
                if has(i, -2):
                    pq, pj = rel(q, j, -2)
                    wait_alone(pool, s_rt, NRT * (n - 2) + NRT)
                    pool.wait_ge(s_init, 16 * (E + 1))
                    for k in range(2):
                        for t in range(TB):
                            g.indirect_dma_start(
                                out=rows, out_offset=bass.IndirectOffsetOnAxis(ap=sli[:, k, t:t + 1], axis=0),
                                in_=rowi[:, pj % 2, t, :], in_offset=None, bounds_check=NSLOTS - 1,
                                oob_is_err=False).then_inc(s_send[pj % 2], 16)
                if has(i, 2):
                    ln1_h(*rel(q, j, 2))
                if i == 14:
                    all_max(0, 0)
                if has(i, -2):
                    wait(pool, s_send[pj % 2], 2 * TB * 16 * (2 * pq + pj // 2 + 1))
                    pool.sem_inc(s_sent, 1)

            def all_max(e, which):
                wait_alone(pool, s_wch, WLINKS * e + (16 if which else 7))
                g.partition_all_reduce(wmg[:, which:which + 1], wmx[:, 5:6], P, ABSMAX).then_inc(s_wall, 1)

            ln1_h(0, 0)
            ln1_norm(0)
            ln1_h(0, 1)
            attn_steps(pool, step)

            with pool.Fori(0, E) as e:
                for u in range(2):
                    all_max(e + u, 1 - u)
                    for t in range(UT):
                        i = UT * u + t
                        wait_alone(pool, s_yo, 2 * UT * e + i + 1)
                        g.indirect_dma_start(
                            out=out, out_offset=bass.IndirectOffsetOnAxis(ap=midx[:, u, t:t + 1], axis=0),
                            in_=yo[:, i % 2, :], in_offset=None, compute_op=ALU.add).then_inc(s_add[i % 2], 16)
                        wait(pool, s_add[i % 2], 16 * (UT * e + i // 2 + 1))
                        pool.sem_inc(s_added, 1)

        @block.scalar
        def _(act):
            a = nc.scalar
            act.sem_inc(s_hhi, 4)
            act.wait_ge(s_small, 48)
            a.activation(csig[:, :, :], cts[:, :, :], ACT.Sigmoid).then_inc(s_csig, 1)

            def square(n):
                for t in range(TB):
                    wait(act, s_ha1, TB * n + t + 1)
                    wait(act, s_sq, TB * n + t)
                    a.activation(junk[:, :], h1[:, t, :], ACT.Square, scale=float(D) ** -0.5,
                                 accum_out=ss1[:, t:t + 1]).then_inc(s_sq, 1)

            def norm(n):
                wait(act, s_rn, n + 1)
                for t in range(TB):
                    a.activation(h1[:, t, :], h1[:, t, :], ACT.Copy, scale=rn1[:, t:t + 1]).then_inc(s_xn, 1)

            def hi1(n, j, c):
                wait(act, s_t1, KC * n + c + 1)
                a.activation(xns[:, j % 2, 0, c, :], bank_t[c % 2][:, :], ACT.Copy,
                             scale=gams[:, c:c + 1]).then_inc(s_xhi, 1)

            act.wait_ge(s_dch, START_LINKS)
            act.wait_ge(s_wqraw, 16)
            for c in range(KC):
                a.activation(wqs[:, 0, c, :], wq_raw[:, c, :], ACT.Copy, scale=sc0[:, 0:1]).then_inc(s_wqhi, 1)
            square(0)
            norm(0)
            for c in range(KC):
                hi1(0, 0, c)

            def sigmoid(n, c):
                wait(act, s_qkv, 12 * n + 3 * c + 1)
                wait(act, s_scn, KC * n + c - 1)
                a.activation(sig[:, c % 2, :], bank_a[:, :], ACT.Sigmoid, scale=iq[:, 0:1]).then_inc(s_sig, 1)

            def step(q, j, i):
                n = 4 * q + j
                if has(i, 0):
                    sigmoid(n, 0)
                if has(i, 1):
                    square(n + 1)
                if has(i, 1):
                    norm(n + 1)
                if has(i, -2):
                    wait(act, s_rt, NRT * (n - 2) + 3)
                    a.activation(prb[:, :, :], lgt[:, :, :], ACT.Exp).then_inc(s_ex, 1)
                if has(i, 0):
                    sigmoid(n, 1)
                for c in range(KC):
                    if has(i, 1):
                        hi1(n + 1, j + 1, c)
                    if c == 2 and has(i, 0):
                        sigmoid(n, 2)
                if has(i, -1):
                    pq, pj = rel(q, j, -1)
                    wait(act, s_sent, n - 1)
                    for t in range(TB):
                        wait(act, s_ha2, TB * (n - 1) + t + 1)
                        a.activation(row[:, pj % 2, t, 0:D], h2[:, t, :], ACT.Copy).then_inc(s_rhi, 1)
                for t in range(TB):
                    if has(i, -1):
                        wait(act, s_t3, TB * (n - 1) + t + 1)
                        wait(act, s_lg, TB * (n - 1) + t - 1)
                        a.activation(h2T[:, t % 2, :, :], bank_t16[t % 2], ACT.Copy).then_inc(s_ht, 1)
                    if t == 1 and has(i, 0):
                        sigmoid(n, 3)
                if i == 15:
                    w_hi(0, 0)

            def w_hi(e, which):
                dst = w1s if which == 0 else w2s
                for c in range(4):
                    wait(act, s_wch, WLINKS * e + (20 if which else 11))
                    if which == 0:
                        wait(act, s_mm1, 4 * HC * e)
                        d = dst[:, 0, c, :]
                    else:
                        wait(act, s_mm2, 2 * UT * e + 1)
                        d = dst[:, 0, 4 * c:4 * c + 4, :].rearrange("p c d -> p (c d)")
                    a.activation(d, stage[:, c, :], ACT.Copy, scale=wsc[:, which:which + 1]).then_inc(s_whi, 1)

            attn_steps(act, step)

            with act.Fori(0, E) as e:
                for u in range(2):
                    v = 2 * e + u
                    wait(act, s_b1s, e + 1)
                    for i in range(2 * HC):
                        hb, b = i // 2, i % 2
                        wait(act, s_mm1, 2 * HC * v + i + 1)
                        wait(act, s_hlo, 2 * HC * v + i + 1)
                        bias = b1s[:, 2 * u + b, hb:hb + 1]
                        src = bank_h[i % 4][:, 0:CAP]
                        a.activation(rt[:, i % 4, :], src, ACT.Relu, bias=bias, scale=HID_SHIFT).then_inc(s_r, 1)
                        a.activation(hid[:, 0, hb, b * CAP:(b + 1) * CAP], src, ACT.Relu, bias=bias,
                                     scale=HID_SHIFT).then_inc(s_hhi, 1)
                        if u == 0 and i == 21:
                            w_hi(e, 1)
                w_hi(e + 1, 0)

        @block.vector
        def _(dve):
            v_ = nc.vector
            links = [0]

            def link(ins):
                links[0] += 1
                ins.then_inc(s_dch, 1)
                dve.wait_ge(s_dch, links[0])

            dve.sem_inc(s_hlo, 4)
            dve.sem_inc(s_yd, 2)
            for e in range(E):
                v_.memset(rev[:, :, e:e + 1], float(E - e)).then_inc(s_cd, 1)
                v_.memset(base[:, e:e + 1], float(e * SLOTS)).then_inc(s_cd, 1)
            v_.memset(cm[:, :], 0.0).then_inc(s_cd, 1)
            v_.memset(ecur[:, :], 0.0).then_inc(s_cd, 1)
            v_.memset(ones[:, :], 1.0).then_inc(s_cd, 1)
            v_.memset(modr[0:B, 6 * D:MODW], 0.0).then_inc(s_cd, 1)
            dve.wait_ge(s_const, 4)
            v_.tensor_copy(idf[:, :], idi[:, :]).then_inc(s_cd, 1)
            dve.wait_ge(s_const, 6)
            v_.tensor_copy(zrow[:, :].bitcast(F32)[:, META + 3:META + 4], zid[:, :]).then_inc(s_zrow, 1)

            def bn(n, j, src, st, s, s_in, base_in):
                for t in range(TB):
                    wait(dve, s_in, base_in(t))
                    v_.bn_stats(st[:, t, :], src[:, j, t, :]).then_inc(s, 1)

            def stats(n, st, sm, s_bn, s_l):
                me, mo, ve, vo = (st[:, :, k:k + 1].rearrange("p t a -> p (t a)") for k in (1, 4, 2, 5))
                k = [0]

                def lk(ins):
                    k[0] += 1
                    ins.then_inc(s_l, 1)
                    wait(dve, s_l, 7 * n + k[0])
                wait(dve, s_bn, TB * n + TB)
                v_.tensor_tensor(sm[:, 0, :], me, mo, ALU.add).then_inc(s_l, 1)
                v_.tensor_tensor(sm[:, 1, :], me, mo, ALU.subtract).then_inc(s_l, 1)
                k[0] = 2
                lk(v_.tensor_tensor(sm[:, 2, :], ve, vo, ALU.add))
                v_.tensor_scalar(sm[:, 4, :], sm[:, 0, :], 0.5, None, ALU.mult).then_inc(s_l, 1)
                k[0] += 1
                lk(v_.scalar_tensor_tensor(sm[:, 3, :], sm[:, 1, :], 0.25, sm[:, 1, :], ALU.mult, ALU.mult))
                lk(v_.scalar_tensor_tensor(sm[:, 2, :], sm[:, 2, :], 1.0 / D, sm[:, 3, :], ALU.mult, ALU.add))
                v_.tensor_scalar(sm[:, 5, :], sm[:, 2, :], 1e-5, None, ALU.add).then_inc(s_l, 1)

            def z(n, j, h, src, sm, rs, s_r, s_zz):
                wait(dve, s_r, n + 1)
                for t in range(TB):
                    v_.tensor_scalar(h[:, t, :], src[:, j, t, :], sm[:, 4, t:t + 1], rs[:, t:t + 1],
                                     ALU.subtract, ALU.mult).then_inc(s_zz, 1)

            def ln1(q, j):
                n = 4 * q + j
                bn(n, j, xbuf, st1, s_bn1, s_x[j], lambda t: 16 * (q + 1))
                stats(n, st1, sm1, s_bn1, s_l1)
                wait(dve, s_t1, KC * n)
                z(n, j, h1, xbuf, sm1, rs1, s_r1, s_z1)

            def clamp_norm(n):
                wait(dve, s_rp, n + 1)
                v_.tensor_scalar(rn1[:, :], rp1[:, :], float(D) ** 0.5 * 1e12, None, ALU.min).then_inc(s_rn, 1)

            def lo1(n, j, c):
                wait(dve, s_xhi, KC * n + c + 1)
                v_.scalar_tensor_tensor(xns[:, j % 2, 1, c, :], bank_t[c % 2][:, :], gams[:, c:c + 1],
                                        xns[:, j % 2, 0, c, :], ALU.mult, ALU.subtract).then_inc(s_xlo, 1)

            def pow2(lk, mx, ex, s_out, i_out):
                lk(v_.tensor_scalar(mx, mx, TINY, None, ALU.max))
                lk(v_.tensor_scalar(ex.bitcast(I32), mx.bitcast(I32), EXPONENT, None, ALU.bitwise_and))
                lk(v_.tensor_scalar(s_out.bitcast(I32), ex.bitcast(I32), -1.0, float((254 + KEXP) << 23),
                                    ALU.mult, ALU.add))
                lk(v_.tensor_scalar(i_out.bitcast(I32), ex.bitcast(I32), float(-(KEXP << 23)), None, ALU.add))

            dve.wait_ge(s_small, 48)
            v_.tensor_reduce(mx0[:, 1:2], wrr[:, :, :].rearrange("p c e -> p (c e)"), AX, ALU.max,
                             apply_absolute_value=True).then_inc(s_max0, 1)
            v_.tensor_reduce(mx0[:, 2:3], gam[:, :], AX, ALU.max, apply_absolute_value=True).then_inc(s_max0, 1)
            dve.wait_ge(s_csig, 1)
            v_.tensor_tensor(silc[:, :, :], csig[:, :, :], cts[:, :, :], ALU.mult).then_inc(s_silc, 1)
            bn(0, 0, xbuf, st1, s_bn1, s_x[0], lambda t: 16)
            stats(0, st1, sm1, s_bn1, s_l1)
            for m in range(6):
                dve.wait_ge(s_modmm, m + 1)
                dst = modr[0:B, m * D:(m + 1) * D]
                if m in (1, 4):
                    link(v_.tensor_scalar(dst, bank[m][0:B, :], 1.0, None, ALU.add))
                else:
                    link(v_.tensor_copy(dst, bank[m][0:B, :]))
            for m in (2, 5):
                gsrc = modr[0:B, m * D:(m + 1) * D]
                link(v_.tensor_scalar(modt[0:B, 0:D], gsrc, 0.0, 2.0, ALU.is_ge, ALU.mult))
                link(v_.scalar_tensor_tensor(modt[0:B, D:2 * D], gsrc, -1.0, gsrc, ALU.mult, ALU.max))
                link(v_.tensor_scalar(modt[0:B, D:2 * D], modt[0:B, D:2 * D], 0.25, None, ALU.max))
                link(v_.scalar_tensor_tensor(gsrc, modt[0:B, 0:D], -1.0, modt[0:B, D:2 * D], ALU.add, ALU.mult))
            scb = modr[0:B, 3 * D:5 * D]
            shc = modr[0:B, 6 * D:6 * D + 1]
            link(v_.tensor_reduce(mrow[0:B, 0:1], scb, AX, ALU.max, apply_absolute_value=True))
            pow2(link, mrow[0:B, 0:1], mrow[0:B, 1:2], shc, modr[0:B, 6 * D + 1:6 * D + 2])
            link(v_.tensor_scalar(scb, scb, shc, None, ALU.mult))
            assert links[0] == MOD_LINKS
            dve.wait_ge(s_wqraw, 16)
            v_.tensor_reduce(mx0[:, 0:1], wq_raw.rearrange("p c e -> p (c e)"), AX, ALU.max,
                             apply_absolute_value=True).then_inc(s_max0, 1)
            dve.wait_ge(s_max0, 4)
            pow2(link, mg0[:, 0:3], ex0[:, 0:3], sc0[:, 0:3], is0[:, 0:3])
            link(v_.tensor_scalar(gams[:, :], gam[:, :], sc0[:, 2:3], None, ALU.mult))
            link(v_.tensor_tensor(iq[:, 0:1], is0[:, 0:1], is0[:, 2:3], ALU.mult))
            link(v_.tensor_tensor(iq[:, 1:2], iq[:, 0:1], iq[:, 0:1], ALU.mult))
            link(v_.tensor_scalar(wrs[:, 0, :, :], wrr[:, :, :], sc0[:, 1:2], None, ALU.mult))
            link(v_.scalar_tensor_tensor(wrs[:, 1, :, :], wrr[:, :, :], sc0[:, 1:2], wrs[:, 0, :, :],
                                         ALU.mult, ALU.subtract))
            assert links[0] == START_LINKS
            z(0, 0, h1, xbuf, sm1, rs1, s_r1, s_z1)
            for c in range(KC):
                dve.wait_ge(s_wqhi, c + 1)
                v_.scalar_tensor_tensor(wqs[:, 1, c, :], wq_raw[:, c, :], sc0[:, 0:1], wqs[:, 0, c, :],
                                        ALU.mult, ALU.subtract).then_inc(s_wqlo, 1)
            dve.wait_ge(s_gat, 1)
            v_.tensor_scalar(gaS[:, :, :], bank[6][:, 0:KC * B].rearrange("p (c b) -> p c b", c=KC), iq[:, 1:2],
                             None, ALU.mult).then_inc(s_cga, 1)
            dve.wait_ge(s_shb, 16)
            link(v_.tensor_scalar(irT[:, :], shb[:, :, 1], is0[:, 1:2], None, ALU.mult))
            link(v_.tensor_scalar(shb9[:, :], shb[:, :, 0], HID_SHIFT, None, ALU.mult))
            link(v_.tensor_reduce(shmax[:, :], shb[:, :, 0], AX, ALU.max))
            link(v_.tensor_scalar(shmax[:, :], shmax[:, :], B1_SHIFT, None, ALU.mult))
            for w in range(2):
                for k, (p0, p1, b) in ((0, (0, P, 0)), (1, (0, P // 2, 0)), (1, (P // 2, P, 1)), (2, (0, P, 1))):
                    link(v_.tensor_scalar(ishk[p0:p1, w, k:k + 1], shb[p0:p1, 2 * w + b, 1:2], 1.0 / HID_SHIFT, None,
                                          ALU.mult))
            clamp_norm(0)
            for c in range(KC):
                lo1(0, 0, c)
            ln1(0, 1)

            def mix(q, j, c):
                n = 4 * q + j
                k = KC * n + c
                wait(dve, s_sig, k + 1)
                wait(dve, s_qkv, 12 * n + 3 * c + 2)
                wait(dve, s_y, k - 1)
                v_.tensor_tensor_scan(scn[:, c % 2, :], sig[:, c % 2, :], bank_kv[c % 2][:, :],
                                      0.0 if j == 0 else carry[:, c:c + 1], ALU.mult, ALU.add).then_inc(s_scn, 1)
                wait(dve, s_scn, k + 1)
                v_.tensor_copy(carry[:, c:c + 1], scn[:, c % 2, BLK - 1:BLK]).then_inc(s_car, 1)
                wait(dve, s_qkv, 12 * n + 3 * c + 3)
                wait(dve, s_t2, TB * n)
                v_.scalar_tensor_tensor(yT[:, c, :], bank_q[c % 2][:, :], cga[:, c:c + 1], scn[:, c % 2, :],
                                        ALU.mult, ALU.mult).then_inc(s_y, 1)
                wait(dve, s_car, k + 1)

            def lo2(n, j, t):
                wait(dve, s_rhi, TB * n + t + 1)
                v_.tensor_tensor(row[:, j % 2, t, D:2 * D], h2[:, t, :], row[:, j % 2, t, 0:D],
                                 ALU.subtract).then_inc(s_rlo, 1)

            def rlink(n, k):
                def lk(ins):
                    k[0] += 1
                    ins.then_inc(s_rt, 1)
                    wait(dve, s_rt, NRT * n + k[0])
                return lk

            def bc(ap):
                return ap.unsqueeze(2).to_broadcast([P, TB, E])

            def route_choose(q, j):
                n = 4 * q + j
                lk = rlink(n, [0])
                wait(dve, s_lg, TB * n + TB)
                lk(v_.tensor_scalar(lgt[:, :, :], bank_r[:, 0:TB * E].rearrange("p (t e) -> p t e", t=TB),
                                    ir[:, 0:1], None, ALU.mult))
                lk(v_.tensor_reduce(rv[:, 0, :], lgt[:, :, :], AX, ALU.max))
                lk(v_.tensor_tensor(lgt[:, :, :], lgt[:, :, :], bc(rv[:, 0, :]), ALU.subtract))
                wait(dve, s_ex, n + 1)
                lk(v_.tensor_reduce(rv[:, 1, :], prb[:, :, :], AX, ALU.add))
                lk(v_.reciprocal(rv[:, 2, :], rv[:, 1, :]))
                lk(v_.tensor_tensor(prb[:, :, :], prb[:, :, :], bc(rv[:, 2, :]), ALU.mult))
                for src, best, first, oh in ((prb, 3, 4, oh1), (prm, 5, 6, oh2)):
                    lk(v_.tensor_reduce(rv[:, best, :], src[:, :, :], AX, ALU.max))
                    lk(v_.tensor_tensor(eqt[:, :, :], src[:, :, :], bc(rv[:, best, :]), ALU.is_equal))
                    lk(v_.tensor_tensor(wgt[:, :, :], eqt[:, :, :], rev[:, :, :], ALU.mult))
                    lk(v_.tensor_reduce(rv[:, first, :], wgt[:, :, :], AX, ALU.max))
                    lk(v_.tensor_tensor(oh[:, :, :], rev[:, :, :], bc(rv[:, first, :]), ALU.is_equal))
                    if src is prb:
                        lk(v_.scalar_tensor_tensor(prm[:, :, :], oh1[:, :, :], -2.0, prb[:, :, :], ALU.mult, ALU.add))
                lk(v_.tensor_tensor(mh[:, :, :], oh1[:, :, :], oh2[:, :, :], ALU.add))

            def route_place(q, j):
                n = 4 * q + j
                lk = rlink(n, [18])
                wait(dve, s_pos, n + 1)
                pos = bank_r[:, 64:64 + TB * E].rearrange("p (t e) -> p t e", t=TB)
                lk(v_.tensor_scalar(eqt[:, :, :], pos, float(CAP), FAR, ALU.is_ge, ALU.mult))
                lk(v_.tensor_tensor(wgt[:, :, :], pos, base[:, :].unsqueeze(1).to_broadcast([P, TB, E]), ALU.add))
                lk(v_.tensor_tensor(eqt[:, :, :], eqt[:, :, :], wgt[:, :, :], ALU.add))
                wait(dve, s_sent, n + 1)
                for k, oh in enumerate((oh1, oh2)):
                    lk(v_.tensor_tensor(wgt[:, :, :], oh[:, :, :], eqt[:, :, :], ALU.mult))
                    lk(v_.tensor_reduce(slf[:, k, :], wgt[:, :, :], AX, ALU.add))
                lk(v_.tensor_copy(sli[:, :, :], slf[:, :, :]))
                for k in range(2):
                    lk(v_.scalar_tensor_tensor(rowf[:, j % 2, :, META + k], slf[:, k, :], float(NSLOTS),
                                               rv[:, 3 + 2 * k, :], ALU.is_lt, ALU.mult))
                lk(v_.tensor_scalar(rowf[:, j % 2, :, META + 2], rv[:, 4, :], -1.0, float(E), ALU.mult, ALU.add))
                lk(v_.tensor_reduce(cs[:, :], mh[:, :, :].rearrange("p t e -> p e t"), AX, ALU.add))
                if j == BPB - 1:
                    lk(v_.memset(cm[:, :], 0.0))
                    lk(v_.tensor_scalar(base[:, :], base[:, :], float(CAP), None, ALU.add))
                else:
                    lk(v_.tensor_tensor(cm[:, :], cm[:, :], cs[:, :], ALU.add))
                    lk(v_.tensor_scalar(cs[:, :], cs[:, :], 0.0, None, ALU.mult))
                lk(v_.tensor_copy(rowf[:, j % 2, :, META + 3], idf[:, :]))
                lk(v_.tensor_scalar(idf[:, :], idf[:, :], float(BLK), None, ALU.add))

            dve.wait_ge(s_cd, 21)

            def step(q, j, i):
                n = 4 * q + j
                if has(i, -1):
                    pq, pj = rel(q, j, -1)
                    for t in range(TB):
                        wait(dve, s_t2, TB * (n - 1) + t + 1)
                        v_.tensor_tensor(xbuf[:, pj, t, :], xbuf[:, pj, t, :], bank_t[t % 2][:, :],
                                         ALU.add).then_inc(s_x2, 1)
                    bn(n - 1, pj, xbuf, st2, s_bn2, s_x2, lambda t: TB * (n - 1) + t + 1)
                    stats(n - 1, st2, sm2, s_bn2, s_l2)
                if has(i, 1):
                    clamp_norm(n + 1)
                if has(i, 0) and j == 0:
                    v_.tensor_copy(cga[:, :], gaS[:, :, bass.ds(q, 1)].rearrange("p c a -> p (c a)")).then_inc(s_cga, 1)
                    wait(dve, s_cga, 2 * q + 2)
                if has(i, -2) and j == 2:
                    v_.tensor_copy(ir[:, :], irT[:, bass.ds(q, 1)]).then_inc(s_cga, 1)
                    wait(dve, s_cga, 2 * q + 3)
                if has(i, 0):
                    mix(q, j, 0)
                if has(i, -2):
                    pq, pj = rel(q, j, -2)
                    route_choose(pq, pj)
                if has(i, -1):
                    z(n - 1, pj_of(j), h2, xbuf, sm2, rs2, s_r2, s_z2)
                if has(i, 0):
                    mix(q, j, 1)
                if has(i, 1):
                    for c in range(KC):
                        lo1(n + 1, j + 1, c)
                if has(i, -2):
                    route_place(pq, pj)
                for t in range(TB):
                    if t == 2 and has(i, 0):
                        mix(q, j, 2)
                    if has(i, -1):
                        lo2(n - 1, j - 1, t)
                if i == 14:
                    for c in range(4):
                        w_max_quarter(0, 0, c)
                    w_scale(0, 0)
                    b1_scale(0)
                if i == 15:
                    for c in range(4):
                        w_lo(0, 0, c)
                if has(i, 2):
                    ln1(*rel(q, j, 2))
                if has(i, 0):
                    mix(q, j, 3)

            def pj_of(j):
                return (j - 1) % 4

            def w_link(e, which, k, ins):
                ins.then_inc(s_wch, 1)
                wait(dve, s_wch, WLINKS * e + 11 * which + k)

            def w_max_quarter(e, which, c):
                wait(dve, s_stg[c], 16 * (2 * e + which + 1))
                v_.tensor_reduce(wmx[:, c:c + 1], stage[:, c, :], AX, ALU.max,
                                 apply_absolute_value=True).then_inc(s_wch, 1)

            def w_scale(e, which):
                k = [4]

                def lk(ins):
                    k[0] += 1
                    w_link(e, which, k[0], ins)
                if which == 0:
                    wait(dve, s_b1, 16 * (e + 1))
                    lk(v_.tensor_reduce(wmx[:, 6:7], b1r[:, :], AX, ALU.max, apply_absolute_value=True))
                    lk(v_.tensor_scalar(wmx[:, 4:5], wmx[:, 6:7], shmax[:, 0:1], None, ALU.mult))
                else:
                    wait(dve, s_wch, WLINKS * e + 11 * which + 4)
                lk(v_.tensor_reduce(wmx[:, 5:6], wmx[:, 0:5 - which], AX, ALU.max))
                wait(dve, s_wall, 2 * e + which + 1)
                pow2(lk, wmg[:, which:which + 1], wex[:, which:which + 1], wsc[:, which:which + 1],
                     wis[:, which:which + 1])
                if which == 1:
                    v_.tensor_scalar(inv2[:, :, :], ishk[:, :, :], wis[:, 0:1], wis[:, 1:2],
                                     ALU.mult, ALU.mult).then_inc(s_inv, 1)

            def b1_scale(e):
                wait(dve, s_hhi, 4 * HC * e + 4)
                for b in range(B):
                    ins = v_.tensor_scalar(b1s[:, b, :], b1r[:, :], wsc[:, 0:1], shb9[:, b:b + 1], ALU.mult, ALU.mult)
                ins.then_inc(s_b1s, 1)

            def w_lo(e, which, c):
                wait(dve, s_whi, 8 * e + 4 * which + c + 1)
                if which == 0:
                    hi, lo = w1s[:, 0, c, :], w1s[:, 1, c, :]
                else:
                    hi, lo = (w2s[:, s, 4 * c:4 * c + 4, :].rearrange("p c d -> p (c d)") for s in range(2))
                v_.scalar_tensor_tensor(lo, stage[:, c, :], wsc[:, which:which + 1], hi,
                                        ALU.mult, ALU.subtract).then_inc(s_wlo, 1)

            def turned(v, u, t):
                wait(dve, s_tg, UT * v + t + 1)
                v_.tensor_copy(xT[:, u, :, t * P:(t + 1) * P], bank_t16[(u + t) % 2]).then_inc(s_xt, 1)

            def take_meta(v, u):
                wait(dve, s_g, 16 * (v + 1))
                v_.tensor_copy(midx[:, u, :], growf[:, :, META + 3])
                v_.tensor_copy(meta[:, u, :, :], growf[:, :, META:META + 3]).then_inc(s_meta, 1)

            def outputs(e, u, t):
                i = UT * u + t
                kind = 0 if t < 2 else 1 if t == 2 else 2
                wait(dve, s_mm2, 2 * UT * e + i + 2)
                wait(dve, s_gate, 7 * e + 3 * u + 3)
                if u == 0 and t == 0:
                    wait(dve, s_inv, e + 1)
                    wait(dve, s_b2, 16 * (e + 1))
                    dve.wait_ge(s_gb, 16 * 8)
                v_.scalar_tensor_tensor(yv[:, i % 2, :], bank_y[i % 2][:, :], inv2[:, u, kind:kind + 1], b2t,
                                        ALU.mult, ALU.add).then_inc(s_yd, 1)
                wait(dve, s_yd, 2 * UT * e + i + 3)
                wait(dve, s_added, 2 * UT * e + i + 1)
                v_.scalar_tensor_tensor(yo[:, i % 2, :], yv[:, i % 2, :], gt[:, 2, t:t + 1], gbt[:, u, kind, :],
                                        ALU.mult, ALU.mult).then_inc(s_yo, 1)

            attn_steps(dve, step)
            take_meta(0, 0)
            for t in range(UT):
                turned(0, 0, t)
            with dve.Fori(0, E) as e:
                for u in range(2):
                    v = 2 * e + u
                    wait(dve, s_meta, v + 1)
                    v_.scalar_tensor_tensor(gt[:, 0, :], meta[:, u, :, 2], ecur[:, 0:1], meta[:, u, :, 0],
                                            ALU.is_equal, ALU.mult).then_inc(s_gate, 1)
                    v_.scalar_tensor_tensor(gt[:, 1, :], meta[:, u, :, 2], ecur[:, 0:1], meta[:, u, :, 1],
                                            ALU.not_equal, ALU.mult).then_inc(s_gate, 1)
                    wait(dve, s_gate, 7 * e + 3 * u + 2)
                    v_.tensor_tensor(gt[:, 2, :], gt[:, 0, :], gt[:, 1, :], ALU.add).then_inc(s_gate, 1)
                    for i in range(2 * HC):
                        hb, b = i // 2, i % 2
                        cols = slice(b * CAP, (b + 1) * CAP)
                        wait(dve, s_hhi, 2 * HC * v + i + 5)
                        v_.tensor_tensor(hid[:, 1, hb, cols], rt[:, i % 4, :], hid[:, 0, hb, cols],
                                         ALU.subtract).then_inc(s_hlo, 1)
                        if i in (8, 11, 14, 17):
                            w_max_quarter(e + u, 1 - u, (i - 8) // 3)
                        if i == 19:
                            w_scale(e + u, 1 - u)
                        if u == 0 and i in (22, 24, 26, 28):
                            w_lo(e, 1, (i - 22) // 2)
                    if u == 1:
                        b1_scale(e + 1)
                    for t in range(UT):
                        outputs(e, u, t)
                        if t == 1:
                            take_meta(v + 1, 1 - u)
                        turned(v + 1, 1 - u, t)
                        if u == 1 and t < 4:
                            w_lo(e + 1, 0, t)
                wait(dve, s_gate, 7 * e + 6)
                v_.tensor_scalar(ecur[:, :], ecur[:, :], 1.0, None, ALU.add).then_inc(s_gate, 1)
                wait(dve, s_gate, 7 * e + 7)

        @block.tensor
        def _(pe):
            mm, tr = nc.tensor.matmul, nc.tensor.transpose
            pe.sem_inc(s_mm2, 1)
            pe.wait_ge(s_silc, 1)
            for m in range(6):
                wm = (stage[:, m, :] if m < 4 else wmod_hi[:, m - 4, :]).rearrange("p (c n) -> p c n", c=KC)
                pe.wait_ge(s_wmod[m], 16)
                for c in range(KC):
                    ins = mm(bank[m][0:B, :], silc[:, c, :], wm[:, c, :], start=c == 0, stop=c == KC - 1)
                ins.then_inc(s_modmm, 1)
            pe.wait_ge(s_dch, MOD_LINKS)
            pe.wait_ge(s_const, 10)
            for c in range(KC):
                ins = tr(bank[6][:, c * B:(c + 1) * B], modr[0:B, 2 * D + c * P:2 * D + (c + 1) * P], ident32[0:B, 0:B])
            ins.then_inc(s_gat, 1)

            def turn_xn(q, j, c, i):
                n = 4 * q + j
                wait(pe, s_xn, TB * n + TB)
                if i == -1:
                    pe.wait_ge(s_cga, 1)
                    wait(pe, s_xlo, c - 1)
                elif c >= 2:
                    wait(pe, s_xlo, KC * n + c - 1)
                elif i == 0:
                    wait(pe, s_xlo, KC * (n - 1) + c + 3)
                else:
                    wait(pe, s_x2, TB * (n - 2) + c + 3)
                for t in range(TB):
                    ins = tr(bank_t[c % 2][:, t * P:(t + 1) * P], h1[:, t, c * P:(c + 1) * P], ident32[:, :])
                ins.then_inc(s_t1, 1)

            def turn_y(q, j, t, i):
                n = 4 * q + j
                wait(pe, s_y, KC * n)
                if t >= 2:
                    wait(pe, s_x2, TB * (n - 1) + t - 1)
                elif i == 1:
                    wait(pe, s_xlo, KC * n + t + 3)
                else:
                    wait(pe, s_ht, TB * (n - 2) + t + 3)
                for c in range(KC):
                    ins = tr(bank_t[t % 2][:, c * P:(c + 1) * P], yT[:, c, t * P:(t + 1) * P], ident32[:, :])
                ins.then_inc(s_t2, 1)

            def turn_rows(q, j, t, i):
                n = 4 * q + j
                wait(pe, s_rlo, TB * (n - 1) + t + 1)
                if t >= 2:
                    wait(pe, s_ht, TB * (n - 1) + t - 1)
                elif has(i, 1):
                    wait(pe, s_xlo, KC * (n + 1) + t + 3)
                else:
                    wait(pe, s_x2, TB * (n - 1) + t + 3)
                for c in range(8):
                    ins = tr(bank_t16[t % 2][:, c, :], row[:, (j - 1) % 2, t, c * P:(c + 1) * P], ident16[:, :])
                ins.then_inc(s_t3, 1)

            def logits(n, t):
                wait(pe, s_ht, TB * n + t + 1)
                if t == 0:
                    wait(pe, s_rt, NRT * (n - 1) + 20)
                for k, (xs, ws) in enumerate(((0, 0), (0, 1), (1, 0))):
                    for c in range(KC):
                        ins = mm(bank_r[:, t * E:(t + 1) * E], h2T[:, t % 2, 4 * xs + c, :], wrs[:, ws, c, :],
                                 start=k == 0 and c == 0, stop=k == 2 and c == KC - 1)
                ins.then_inc(s_lg, 1)

            def positions(n):
                wait(pe, s_rt, NRT * n + 18)
                for t in range(TB):
                    o = bank_r[:, 64 + t * E:64 + (t + 1) * E]
                    mm(o, upper[:, :], mh[:, t, :], start=True, stop=False)
                    for k in range(t):
                        mm(o, ones[:, :], mh[:, k, :], start=False, stop=False)
                    ins = mm(o, ones[:, :], cm[:, :], start=False, stop=True)
                ins.then_inc(s_pos, 1)

            def qkv(q, j, c, kind):
                n = 4 * q + j
                dst = (bank_a, bank_kv[c % 2], bank_q[c % 2])[kind]
                if kind == 0:
                    wait(pe, s_sig, KC * n + c)
                elif kind == 1:
                    wait(pe, s_scn, KC * n + c - 1)
                else:
                    wait(pe, s_y, KC * n + c - 1)
                e0 = (2 - kind) * D + c * P
                for kc in range(KC):
                    if c == 0 and kind == 0:
                        wait(pe, s_xlo, KC * n + kc + 1)
                    for xs, ws in ((0, 0), (1, 0), (0, 1)):
                        ins = mm(dst[:, :], wqs[:, ws, kc, e0:e0 + P], xns[:, j % 2, xs, kc, :],
                                 start=kc == 0 and xs == 0 and ws == 0, stop=kc == KC - 1 and ws == 1)
                ins.then_inc(s_qkv, 1)

            def step(q, j, i):
                n = 4 * q + j
                xq, xj = rel(q, j, 1)
                for k in range(12):
                    if has(i, 0):
                        qkv(q, j, k // 3, k % 3)
                    if k == 0 and has(i, -2):
                        logits(n - 2, 3)
                    if k < 2 and has(i, -1):
                        turn_y(q, j, 2 * k, i)
                        turn_y(q, j, 2 * k + 1, i)
                    for c in {4: (0,), 5: (1,), 7: (2, 3)}.get(k, ()):
                        if has(i, 1):
                            turn_xn(xq, xj, c, i)
                    if k == 7 and has(i, -2):
                        positions(n - 2)
                    for t in {9: (0, 1), 10: (2,), 11: (3,)}.get(k, ()):
                        if has(i, -1):
                            turn_rows(q, j, t, i)
                    if k >= 9 and has(i, -1):
                        logits(n - 1, k - 9)

            for c in range(KC):
                turn_xn(0, 0, c, -1)
            pe.wait_ge(s_wqlo, KC)
            attn_steps(pe, step)

            def turn_slots(v, u, t):
                wait(pe, s_g, 16 * (v + 1))
                wait(pe, s_xt, UT * v + t - 1)
                for c in range(8):
                    ins = tr(bank_t16[(u + t) % 2][:, c, :], grow[:, t, c * P:(c + 1) * P], ident16[:, :])
                ins.then_inc(s_tg, 1)

            for t in range(UT):
                turn_slots(0, 0, t)
            with pe.Fori(0, E) as e:
                for u in range(2):
                    v = 2 * e + u
                    wait(pe, s_wlo, 8 * e + 4)
                    wait(pe, s_xt, UT * (v + 1))
                    for hb in range(HC):
                        for kc in range(KC):
                            for ws, xs in ((0, 0), (0, 1), (1, 0)):
                                for b in range(2):
                                    i = 2 * hb + b
                                    if kc == 0 and ws == 0 and xs == 0:
                                        wait(pe, s_hhi, 2 * HC * v + i + 1)
                                    ins = mm(bank_h[i % 4][:, 0:CAP], w1s[:, ws, kc, hb * P:(hb + 1) * P],
                                             xT[:, u, 4 * xs + kc, b * CAP:(b + 1) * CAP],
                                             start=kc == 0 and ws == 0 and xs == 0, stop=kc == KC - 1 and ws == 1)
                                    if kc == KC - 1 and ws == 1:
                                        ins.then_inc(s_mm1, 1)
                    for t in range(UT):
                        i = UT * u + t
                        wait(pe, s_yd, 2 * UT * e + i + 1)
                        for hc in range(HC):
                            if t == 0:
                                wait(pe, s_hlo, 2 * HC * v + 2 * hc + 6)
                                if u == 0 and hc % 4 == 0:
                                    wait(pe, s_wlo, 8 * e + 4 + hc // 4 + 1)
                            for hs, ws in ((0, 0), (0, 1), (1, 0)):
                                ins = mm(bank_y[i % 2][:, :], hid[:, hs, hc, t * P:(t + 1) * P], w2s[:, ws, hc, :],
                                         start=hc == 0 and hs == 0 and ws == 0, stop=hc == HC - 1 and hs == 1)
                        ins.then_inc(s_mm2, 1)
                        turn_slots(v + 1, 1 - u, t)


def kernel(**inputs):
    import numpy as np
    import concourse.bacc as bacc
    from concourse import mybir as mb
    from concourse.bass_utils import run_bass_kernel_spmd as run

    f = {k: np.ascontiguousarray(v) for k, v in inputs.items()}
    laid = {
        "x": f["L0_attn_x"],
        "gamma": np.ascontiguousarray(f["L0_attn_gamma"].reshape(KC, P).T),
        "wq": np.ascontiguousarray(f["L0_attn_w_qkva"].T),
        "wr": np.ascontiguousarray(f["L0_ffn_Wr"].reshape(KC, P, E).transpose(1, 0, 2)),
        "w1": f["L0_ffn_W1"],
        "b1": np.ascontiguousarray(f["L0_ffn_b1"].reshape(E, HC, P).transpose(0, 2, 1)),
        "w2": f["L0_ffn_W2"],
        "b2": f["L0_ffn_b2"],
        "ct": np.ascontiguousarray(f["L0_c"].reshape(B, KC, P).transpose(2, 1, 0)),
        "wmod": f["L0_wmod"],
    }
    nc = bacc.Bacc("TRN2", target_bir_lowering=False, num_devices=1)
    args = [nc.dram_tensor(f"in_{k}", a.shape, mb.dt.from_np(a.dtype), kind="ExternalInput").ap() for k, a in laid.items()]
    out = nc.dram_tensor("out_0_dram", (TOKENS + P, D), mb.dt.float32, kind="ExternalOutput").ap()
    build_program(nc, *args, out)
    r = run(nc, [{f"in_{k}": a for k, a in laid.items()}], core_ids=[0])
    return r.results[0]["out_0_dram"][0:TOKENS].reshape(B, T, D)
```
